# Optimizing a Trainium2 kernel written in Bass

```python
import numpy as np
import jax
import jax.numpy as jnp

def _softmax(x, axis=-1):
    return jax.nn.softmax(x, axis=axis)

def _gelu(x):
    return jax.nn.gelu(x, approximate=True)

def _silu(x):
    return jax.nn.silu(x)

def _sigmoid(x):
    return jax.nn.sigmoid(x)

def _layernorm(x, axis=-1, eps=1e-05):
    m = jnp.mean(x, axis=axis, keepdims=True)
    v = jnp.var(x, axis=axis, keepdims=True)
    return (x - m) / jnp.sqrt(v + eps)

def _scatter_add(tgt, idx, src, axis=0):
    return tgt.at[idx].add(src)

def _segment_sum(src, seg, n):
    return jax.ops.segment_sum(src, seg, n)
kernel_name = 'mk_gnn_resnorm_d4_gnn_r16_31638f'

def setup_inputs(seed: int=0):
    np.random.seed(seed)
    _w = jnp.asarray

    def _rec_inputs():
        import jax
        import jax.numpy as jnp
        _gk = jax.random.key(seed)
        x = -0.0003713 + 1 * jax.random.normal(jax.random.fold_in(_gk, 1), (6250, 128), jnp.float32)
        src = jax.random.randint(jax.random.fold_in(_gk, 2), (200000,), 0, 6250, jnp.int32)
        dst = jnp.minimum((6250 * jax.random.uniform(jax.random.fold_in(_gk, 3), (200000,)) ** 2.0).astype(jnp.int32), 99999)
        _o = jnp.argsort(dst, stable=True)
        src = src[_o]
        dst = dst[_o]
        return (x, src, dst)
    x, src, dst = _rec_inputs()

    def _L0_gnn_setup():
        import jax, jax.numpy as jnp
        import numpy as np
        N_NODES = 6250
        N_EDGES = 100000
        IN_FEATS = 128
        OUT_FEATS = 128
        key = jax.random.key(seed)
        k1, k2, k3, k4, k5, k6 = jax.random.split(key, 6)
        stdv = 1.0 / np.sqrt(OUT_FEATS)
        h = jax.random.normal(k1, (N_NODES, IN_FEATS), dtype=jnp.float32)
        norm = jax.random.uniform(k2, (N_NODES, 1), dtype=jnp.float32)
        weight = jax.random.uniform(k3, (IN_FEATS, OUT_FEATS), dtype=jnp.float32, minval=-stdv, maxval=stdv)
        bias = jax.random.uniform(k4, (OUT_FEATS,), dtype=jnp.float32, minval=-stdv, maxval=stdv)
        src = jax.random.randint(k5, (N_EDGES,), 0, N_NODES, dtype=jnp.int32)
        dst = jax.random.randint(k6, (N_EDGES,), 0, N_NODES, dtype=jnp.int32)
        return {'h': h, 'norm': norm, 'weight': weight, 'bias': bias, 'src': src, 'dst': dst}
    _L0_gnn_all = _L0_gnn_setup()
    _L0_gnn_in = {k: v for k, v in _L0_gnn_all.items() if k in ('weight', 'bias')}
    del _L0_gnn_all

    def _L1_gnn_setup():
        import jax, jax.numpy as jnp
        import numpy as np
        N_NODES = 6250
        N_EDGES = 100000
        IN_FEATS = 128
        OUT_FEATS = 128
        key = jax.random.key(seed)
        k1, k2, k3, k4, k5, k6 = jax.random.split(key, 6)
        feat = jax.random.normal(k1, (N_NODES, IN_FEATS), dtype=jnp.float32)
        src = jax.random.randint(k2, (N_EDGES,), 0, N_NODES, dtype=jnp.int32)
        dst = jax.random.randint(k3, (N_EDGES,), 0, N_NODES, dtype=jnp.int32)
        gain = float(np.sqrt(2.0))
        limit = gain * float(np.sqrt(6.0 / (IN_FEATS + OUT_FEATS)))
        w_neigh = jax.random.uniform(k4, (OUT_FEATS, IN_FEATS), minval=-limit, maxval=limit, dtype=jnp.float32)
        w_self = jax.random.uniform(k5, (OUT_FEATS, IN_FEATS), minval=-limit, maxval=limit, dtype=jnp.float32)
        b_self = jax.random.uniform(k6, (OUT_FEATS,), minval=-0.05, maxval=0.05, dtype=jnp.float32)
        return {'feat': feat, 'w_neigh': w_neigh, 'w_self': w_self, 'b_self': b_self, 'src': src, 'dst': dst}
    _L1_gnn_all = _L1_gnn_setup()
    _L1_gnn_in = {k: v for k, v in _L1_gnn_all.items() if k in ('w_neigh', 'w_self', 'b_self')}
    del _L1_gnn_all

    def _L2_gnn_setup():
        import jax, jax.numpy as jnp
        import numpy as np
        N_NODES = 6250
        N_EDGES = 100000
        IN_DIM = 128
        OUT_DIM = 128
        key = jax.random.key(seed)
        k_x, k_e, k_w1, k_b1, k_w2, k_b2 = jax.random.split(key, 6)
        x = jax.random.normal(k_x, (N_NODES, IN_DIM), dtype=jnp.float32)
        edge_index = jax.random.randint(k_e, (2, N_EDGES), 0, N_NODES, dtype=jnp.int64)
        s1 = 1.0 / np.sqrt(IN_DIM)
        s2 = 1.0 / np.sqrt(OUT_DIM)
        W1 = jax.random.uniform(k_w1, (IN_DIM, OUT_DIM), minval=-s1, maxval=s1, dtype=jnp.float32)
        b1 = jax.random.uniform(k_b1, (OUT_DIM,), minval=-s1, maxval=s1, dtype=jnp.float32)
        W2 = jax.random.uniform(k_w2, (OUT_DIM, OUT_DIM), minval=-s2, maxval=s2, dtype=jnp.float32)
        b2 = jax.random.uniform(k_b2, (OUT_DIM,), minval=-s2, maxval=s2, dtype=jnp.float32)
        return {'x': x, 'edge_index': edge_index, 'W1': W1, 'b1': b1, 'W2': W2, 'b2': b2}
    _L2_gnn_all = _L2_gnn_setup()
    _L2_gnn_in = {k: v for k, v in _L2_gnn_all.items() if k in ('W1', 'b1', 'W2', 'b2')}
    del _L2_gnn_all

    def _L3_gnn_setup():
        import jax, jax.numpy as jnp
        import numpy as np
        N_NODES = 3125
        N_EDGES = 50000
        D_IN = 128
        D_OUT = 128
        key = jax.random.key(seed)
        ks = jax.random.split(key, 6)
        x = jax.random.normal(ks[0], (N_NODES, D_IN), dtype=jnp.float32)
        edge_index = jax.random.randint(ks[1], (2, N_EDGES), 0, N_NODES, dtype=jnp.int32)
        s1 = 1.0 / np.sqrt(2 * D_IN)
        s2 = 1.0 / np.sqrt(D_IN)
        W1 = jax.random.normal(ks[2], (2 * D_IN, D_IN), dtype=jnp.float32) * s1
        b1 = jnp.zeros((D_IN,), dtype=jnp.float32)
        W2 = jax.random.normal(ks[3], (D_IN, 1), dtype=jnp.float32) * s2
        b2 = jnp.zeros((1,), dtype=jnp.float32)
        Wl = jax.random.normal(ks[4], (D_IN, D_OUT), dtype=jnp.float32) * s2
        bl = jnp.zeros((D_OUT,), dtype=jnp.float32)
        return {'x': x, 'edge_index': edge_index, 'W1': W1, 'b1': b1, 'W2': W2, 'b2': b2, 'Wl': Wl, 'bl': bl}
    _L3_gnn_all = _L3_gnn_setup()
    _L3_gnn_in = {k: v for k, v in _L3_gnn_all.items() if k in ('W1', 'b1', 'W2', 'b2', 'Wl', 'bl')}
    del _L3_gnn_all
    return {'x': x, 'src': src, 'dst': dst, 'L0_gnn_weight': _L0_gnn_in['weight'], 'L0_gnn_bias': _L0_gnn_in['bias'], 'L1_gnn_w_neigh': _L1_gnn_in['w_neigh'], 'L1_gnn_w_self': _L1_gnn_in['w_self'], 'L1_gnn_b_self': _L1_gnn_in['b_self'], 'L2_gnn_W1': _L2_gnn_in['W1'], 'L2_gnn_b1': _L2_gnn_in['b1'], 'L2_gnn_W2': _L2_gnn_in['W2'], 'L2_gnn_b2': _L2_gnn_in['b2'], 'L3_gnn_W1': _L3_gnn_in['W1'], 'L3_gnn_b1': _L3_gnn_in['b1'], 'L3_gnn_W2': _L3_gnn_in['W2'], 'L3_gnn_b2': _L3_gnn_in['b2'], 'L3_gnn_Wl': _L3_gnn_in['Wl'], 'L3_gnn_bl': _L3_gnn_in['bl']}

def reference(x, src, dst, L0_gnn_weight, L0_gnn_bias, L1_gnn_w_neigh, L1_gnn_w_self, L1_gnn_b_self, L2_gnn_W1, L2_gnn_b1, L2_gnn_W2, L2_gnn_b2, L3_gnn_W1, L3_gnn_b1, L3_gnn_W2, L3_gnn_b2, L3_gnn_Wl, L3_gnn_bl):
    import jax
    import jax.numpy as jnp

    def _L0_gnn_ref(h, norm, weight, bias, src, dst):
        import jax, jax.numpy as jnp
        import numpy as np
        N_NODES = 6250
        N_EDGES = 100000
        IN_FEATS = 128
        OUT_FEATS = 128
        h = h @ weight
        h = h * norm
        msg = h[src]
        agg = jax.ops.segment_sum(msg, dst, num_segments=N_NODES)
        out = agg * norm + bias
        return jax.nn.relu(out)

    def _L1_gnn_ref(feat, w_neigh, w_self, b_self, src, dst):
        import jax, jax.numpy as jnp
        import numpy as np
        N_NODES = 6250
        N_EDGES = 100000
        IN_FEATS = 128
        OUT_FEATS = 128
        h = jnp.einsum('ni,oi->no', feat, w_neigh)
        msg = h[src]
        summed = jax.ops.segment_sum(msg, dst, num_segments=N_NODES)
        deg = jax.ops.segment_sum(jnp.ones((src.shape[0],), feat.dtype), dst, num_segments=N_NODES)
        h_neigh = summed / jnp.maximum(deg, 1.0)[:, None]
        rst = jnp.einsum('ni,oi->no', feat, w_self) + b_self + h_neigh
        return rst

    def _L2_gnn_ref(x, edge_index, W1, b1, W2, b2):
        import jax, jax.numpy as jnp
        import numpy as np
        N_NODES = 6250
        N_EDGES = 100000
        IN_DIM = 128
        OUT_DIM = 128
        src, dst = (edge_index[0], edge_index[1])
        agg = jax.ops.segment_sum(x[src], dst, num_segments=N_NODES)
        h = x + agg
        h = jax.nn.relu(h @ W1 + b1)
        return h @ W2 + b2

    def _L3_gnn_ref(x, edge_index, W1, b1, W2, b2, Wl, bl):
        import jax, jax.numpy as jnp
        import numpy as np
        N_NODES = 3125
        N_EDGES = 50000
        D_IN = 128
        D_OUT = 128
        row, col = (edge_index[0], edge_index[1])
        n, d = x.shape
        xc = x[row]
        xn = x[col]
        h = jax.nn.relu(xc @ W1[:d] + xn @ W1[d:] + b1)
        mask = jax.nn.sigmoid(h @ W2 + b2)[:, 0]
        seg_sum = jax.ops.segment_sum(mask, row, num_segments=n)
        w = mask / (seg_sum[row] + 1e-09)
        agg = jax.ops.segment_sum(w[:, None] * xn, row, num_segments=n)
        deg = jax.ops.segment_sum(jnp.ones_like(mask), row, num_segments=n)
        out_emb = jnp.where((deg > 0)[:, None], 0.5 * x + 0.5 * agg, x)
        return jax.nn.relu(out_emb @ Wl + bl)
    edge_index = jnp.stack([src, dst])
    deg = jnp.maximum(jax.ops.segment_sum(jnp.ones(dst.shape, jnp.float32), dst, num_segments=6250), 1.0)
    deg_isqrt = deg ** (-0.5)
    x = _layernorm(x + _L0_gnn_ref(x, deg_isqrt[:, None], L0_gnn_weight, L0_gnn_bias, src, dst), axis=-1)
    x = _layernorm(x + _L1_gnn_ref(x, L1_gnn_w_neigh, L1_gnn_w_self, L1_gnn_b_self, src, dst), axis=-1)
    x = _layernorm(x + _L2_gnn_ref(x, edge_index, L2_gnn_W1, L2_gnn_b1, L2_gnn_W2, L2_gnn_b2), axis=-1)
    x = _layernorm(x + _L3_gnn_ref(x, edge_index, L3_gnn_W1, L3_gnn_b1, L3_gnn_W2, L3_gnn_b2, L3_gnn_Wl, L3_gnn_bl), axis=-1)
    return x

_drawn_inputs = setup_inputs


def setup_inputs(seed=0):
    import zlib

    import numpy as np

    out = dict(_drawn_inputs(seed))
    spreads = {'L3_gnn_b1': (0.0, 0.8), 'L3_gnn_bl': (0.0, 0.1)}
    factors = {'L2_gnn_b1': 4.569, 'L3_gnn_W1': 3.647, 'L3_gnn_W2': 4.023}
    for name, (base, spread) in spreads.items():
        noise = np.random.default_rng([zlib.crc32(name.encode()), seed]).standard_normal(out[name].shape)
        drawn = base * np.exp(spread * noise) if base else spread * noise
        out[name] = jnp.asarray(drawn.astype(out[name].dtype))
    for name, factor in factors.items():
        out[name] = (out[name] * factor).astype(out[name].dtype)
    return out
```

```python
import concourse.bass as bass
from concourse import mybir
from contextlib import ExitStack

F32 = mybir.dt.float32
F16 = mybir.dt.float16
BF16 = mybir.dt.bfloat16
I32 = mybir.dt.int32
U16 = mybir.dt.uint16
ALU = mybir.AluOpType
ACT = mybir.ActivationFunctionType
AX = mybir.AxisListType

P = 128
N_NODES = 6250
N_EDGES = 200000
D = 128
NT = -(-N_NODES // P)
NP = NT * P
EC = -(-N_EDGES // P)
LAST = N_EDGES - (P - 1) * EC
SC = 1616
SCD = SC + 1
SCP = 13 * P
DB = 512
NB = -(-NP // DB)
NQ = NB * NT
SPAN = 8192
assert SC >= (N_EDGES // P) + NT and (SC * P - N_EDGES) >= 0 and SCD * P < (1 << 24)


class Chain:

    def __init__(self, eng, sem):
        self.eng, self.sem, self.n, self.loop = eng, sem, 0, None

    def __call__(self, ins):
        ins.then_inc(self.sem, 1)
        self.n += 1
        self.eng.wait_ge(self.sem, self.n if self.loop is None else self.loop + self.n)

    def enter(self, i, per):
        self.loop, self.per = i * per, per

    def leave(self, trips):
        self.n += (trips - 1) * self.per
        self.loop = None


def col(t, i):
    return t[:, bass.ds(i, 1)]


def rank_edges(nc, m, src, dst):
    with ExitStack() as ctx:
        sb = lambda n, s, d: ctx.enter_context(nc.sbuf_tensor(n, s, d))
        sem = lambda n: ctx.enter_context(nc.semaphore(n))
        si, di = sb("src_int", [P, EC], I32), sb("dst_int", [P, EC], I32)
        ti = sb("tile_int", [P, EC], I32)
        key = sb("key", [P, EC], F16)
        hit = sb("hit", [P, EC], F16)
        pos_k = sb("pos_k", [P, EC], F32)
        cnt = sb("lane_count", [P, NT], F32)
        off = sb("lane_offset", [P, NT + 1], F32)
        chi = sb("chunks_int", [P, NT], I32)
        chf = sb("chunks", [P, NT], F32)
        inc = sb("chunks_inclusive", [P, NT], F32)
        pos = m.pos
        ps = ctx.enter_context(nc.psum_tensor("rank_ps", [P, 2, 512], F32))
        s_fill, s_edges, s_const, s_counted, s_sums, s_v, s_pad = (
            sem(n) for n in ("rank_fill", "rank_edges", "rank_const", "rank_counted", "rank_sums", "rank_v", "rank_pad"))
        block = ctx.enter_context(nc.Block())

        @block.sync
        def _(sp):
            sp.wait_ge(s_fill, 2)
            for t, a in ((si, src), (di, dst)):
                for lo, hi in ((0, 112), (112, P - 1)):
                    sp.dma_start(t[lo:hi, :], a[lo * EC:hi * EC].rearrange("(p c) -> p c", c=EC)).then_inc(s_edges, 16)
                sp.dma_start(t[P - 1:P, 0:LAST], a[(P - 1) * EC:N_EDGES].rearrange("(p c) -> p c", p=1)).then_inc(s_edges, 16)
            sp.wait_ge(s_pad, 1)
            sp.dma_start(m.rec.rearrange("(p c) w -> p (c w)", p=P), m.empty[:, 0:2 * SCD]).then_inc(s_edges, 16)
            sp.wait_ge(s_edges, 7 * 16)

        @block.gpsimd
        def _(gp):
            ch = Chain(gp, s_const)
            nc.gpsimd.iota(m.iota512[:, :], pattern=[[1, DB]], base=0, channel_multiplier=0, allow_small_or_imprecise_dtypes=True).then_inc(s_const, 1)
            nc.gpsimd.iota(m.iota128[:, :], pattern=[[1, P]], base=0, channel_multiplier=0, allow_small_or_imprecise_dtypes=True).then_inc(s_const, 1)
            ch.n = 2
            nc.gpsimd.memset(m.empty[:, :], -1.0).then_inc(s_pad, 1)
            ch(nc.gpsimd.memset(m.ones[:, :], 1.0))
            ch(nc.gpsimd.memset(m.zeros16[:, :], 0.0))
            ch(nc.gpsimd.affine_select(out=m.before[:, :], in_=m.ones[:, :], compare_op=ALU.is_gt, fill=0.0, base=0, pattern=[[1, P]], channel_multiplier=-1))
            ch(nc.gpsimd.affine_select(out=m.ident[:, :], in_=m.ones[:, :], compare_op=ALU.is_equal, fill=0.0, base=0, pattern=[[1, P]], channel_multiplier=-1))
            ch(nc.gpsimd.iota(m.neg_tile[:, :].rearrange("p (b t) -> p b t", t=NT), pattern=[[0, NB], [-P, NT]], base=0, channel_multiplier=0, allow_small_or_imprecise_dtypes=True))
            ch(nc.gpsimd.iota(m.neg_block[:, :].rearrange("p (b t) -> p b t", t=NT), pattern=[[-DB, NB], [0, NT]], base=0, channel_multiplier=0, allow_small_or_imprecise_dtypes=True))

        @block.vector
        def _(dve):
            ch = Chain(dve, s_v)
            nc.vector.memset(si[:, :], NT * P).then_inc(s_fill, 1)
            nc.vector.memset(di[:, :], 60 * P).then_inc(s_fill, 1)
            dve.wait_ge(s_const, 8)
            dve.wait_ge(s_edges, 7 * 16)
            nc.vector.tensor_copy(m.pair[:, :, 0], si[:, :])
            nc.vector.tensor_copy(m.pair[:, :, 1], di[:, :])
            ch(nc.vector.tensor_scalar(ti[:, :], si[:, :], 7, None, ALU.arith_shift_right))
            ch(nc.vector.tensor_copy(key[:, :], ti[:, :]))
            ch(nc.vector.tensor_scalar(ti[:, :], di[:, :], 7, None, ALU.arith_shift_right))
            ch(nc.vector.tensor_copy(m.dst_tile[:, :], ti[:, :]))
            ch(nc.vector.scalar_tensor_tensor(m.dst_lo[:, :], m.dst_tile[:, :], -float(P), di[:, :], ALU.mult, ALU.add))
            with dve.Fori(0, NT) as k:
                ch.enter(k, 1)
                ch(nc.vector.tensor_scalar(hit[:, :], key[:, :], col(m.iota128, k), 0.0, ALU.is_equal, ALU.add, accum_out=col(cnt, k)))
                ch.leave(NT)
            nc.vector.tensor_copy(cnt[:, 0:1], cnt[:, 0:1]).then_inc(s_counted, 1)
            dve.wait_ge(s_sums, 1)
            ch(nc.vector.tensor_scalar(chf[:, :], ps[:, 1, 0:NT], float(P - 1), None, ALU.add))
            ch(nc.vector.tensor_copy(chi[:, :], chf[:, :]))
            ch(nc.vector.tensor_scalar(chi[:, :], chi[:, :], 7, None, ALU.arith_shift_right))
            ch(nc.vector.tensor_copy(chf[:, :], chi[:, :]))
            ch(nc.vector.tensor_scalar(chf[:, :], chf[:, :], 1.0, None, ALU.max))
            ch(nc.vector.tensor_tensor_scan(inc[:, :], chf[:, :], chf[:, :], 0.0, ALU.add, ALU.bypass))
            ch(nc.vector.tensor_tensor(m.first_chunk[:, :], inc[:, :], chf[:, :], ALU.subtract))
            ch(nc.vector.scalar_tensor_tensor(off[:, 0:NT], m.first_chunk[:, :], float(P), ps[:, 0, 0:NT], ALU.mult, ALU.add))
            ch(nc.vector.tensor_scalar(off[:, 0:NT], off[:, 0:NT], -1.0, None, ALU.add))
            ch(nc.vector.memset(off[:, NT:NT + 1], float(SC * P - 1)))
            ch(nc.vector.memset(pos[:, :], 0.0))
            with dve.Fori(0, NT + 1) as k:
                ch.enter(k, 4)
                ch(nc.vector.tensor_scalar(hit[:, :], key[:, :], col(m.iota128, k), None, ALU.is_equal))
                ch(nc.vector.tensor_tensor_scan(pos_k[:, :], hit[:, :], hit[:, :], col(off, k), ALU.add, ALU.bypass))
                ch(nc.vector.tensor_tensor(pos_k[:, :], pos_k[:, :], hit[:, :], ALU.mult))
                ch(nc.vector.tensor_tensor(pos[:, :], pos[:, :], pos_k[:, :], ALU.add))
                ch.leave(NT + 1)
            ch(nc.vector.tensor_copy(m.row[:, :], pos[:, :]))
            ch(nc.vector.tensor_scalar(ti[:, :], m.row[:, :], 7, None, ALU.arith_shift_right))
            ch(nc.vector.tensor_scalar(m.row[:, :], m.row[:, :], P - 1, None, ALU.bitwise_and))
            ch(nc.vector.tensor_copy(pos[:, :], m.row[:, :]))
            ch(nc.vector.scalar_tensor_tensor(pos_k[:, :], pos[:, :], float(SCD), ti[:, :], ALU.mult, ALU.add))
            ch(nc.vector.tensor_copy(m.row[:, :], pos_k[:, :]))

        @block.tensor
        def _(pe):
            pe.wait_ge(s_const, 8)
            pe.wait_ge(s_counted, 1)
            nc.tensor.matmul(ps[:, 0, 0:NT], m.before[:, :], cnt[:, :], start=True, stop=True)
            nc.tensor.matmul(ps[:, 1, 0:NT], m.ones[:, :], cnt[:, :], start=True, stop=True).then_inc(s_sums, 1)


def scatter_edges(nc, m):
    G = 8
    FULL, REST = EC // (2 * G), EC % (2 * G)
    with ExitStack() as ctx:
        sb = lambda n, s, d: ctx.enter_context(nc.sbuf_tensor(n, s, d))
        sem = lambda n: ctx.enter_context(nc.semaphore(n))
        row_s = sb("row_stage", [P, 2, G], I32)
        pair_s = sb("pair_stage", [P, 2, G, 2], F32)
        oh_lo = sb("onehot_low", [P, 2, G, P], F16)
        oh_hi = sb("onehot_tile", [P, 2, G, NT], F16)
        ps = ctx.enter_context(nc.psum_tensor("degree_ps", [P, 512], F32))
        s_staged, s_hot, s_hist, s_sent = (sem("sc_" + n) for n in ("staged", "hot", "hist", "sent"))
        s_done = [sem("sc_done0"), sem("sc_done1")]
        block = ctx.enter_context(nc.Block())

        def halves():
            return [(h, G) for h in (0, 1)], [(h, min(G, REST - h * G)) for h in (0, 1) if REST > h * G]

        @block.gpsimd
        def _(gp):
            def send(h, n, turn):
                gp.wait_ge(s_staged, turn + 1)
                gp.sem_inc(s_sent, 1)
                for j in range(n):
                    nc.gpsimd.indirect_dma_start(m.rec, bass.IndirectOffsetOnAxis(ap=row_s[:, h, j:j + 1], axis=0),
                                                 pair_s[:, h, j, :], None).then_inc(s_done[h], 16)
            loop, rest = halves()
            with gp.Fori(0, FULL) as i:
                for h, n in loop:
                    send(h, n, i * 2 + h)
            for h, n in rest:
                send(h, n, 2 * FULL + h)
            for h in (0, 1):
                gp.wait_ge(s_done[h], 16 * (G * FULL + sum(n for g, n in rest if g == h)))

        @block.scalar
        def _(act):
            def stage(h, n, c):
                nc.scalar.activation(row_s[:, h, 0:n], m.row[:, bass.ds(c, n)], ACT.Copy)
                nc.scalar.activation(pair_s[:, h, 0:n, :], m.pair[:, bass.ds(c, n), :], ACT.Copy).then_inc(s_staged, 1)
            loop, rest = halves()
            for h, n in loop:
                stage(h, n, h * G)
            with act.Fori(1, FULL) as i:
                for h, n in loop:
                    act.wait_ge(s_done[h], i * (16 * G))
                    stage(h, n, i * (2 * G) + h * G)
            for h, n in rest:
                act.wait_ge(s_done[h], FULL * 16 * G)
                stage(h, n, FULL * 2 * G + h * G)

        @block.vector
        def _(dve):
            def hot(h, n, c):
                for j in range(n):
                    nc.vector.tensor_scalar(oh_lo[:, h, j, :], m.iota128h[:, :], m.dst_lo[:, bass.ds(c + j, 1)], None, ALU.is_equal)
                    ins = nc.vector.tensor_scalar(oh_hi[:, h, j, :], m.iota128h[:, 0:NT], m.dst_tile[:, bass.ds(c + j, 1)], None, ALU.is_equal)
                ins.then_inc(s_hot, 1)
            loop, rest = halves()
            for h, n in loop:
                hot(h, n, h * G)
            with dve.Fori(1, FULL) as i:
                for h, n in loop:
                    dve.wait_ge(s_hist, i * 2 + (h - 1))
                    hot(h, n, i * (2 * G) + h * G)
            for h, n in rest:
                dve.wait_ge(s_hist, 2 * FULL - 1 + h)
                hot(h, n, FULL * 2 * G + h * G)
            dve.wait_ge(s_hist, 2 * FULL + len(rest))
            nc.vector.tensor_copy(m.deg[:, :], ps[:, 0:NT])

        @block.tensor
        def _(pe):
            def hist(h, n, turn, last=False):
                pe.wait_ge(s_hot, turn + 1)
                for j in range(n):
                    ins = nc.tensor.matmul(ps[:, 0:NT], oh_lo[:, h, j, :], oh_hi[:, h, j, :], start=False, stop=last and j == n - 1)
                ins.then_inc(s_hist, 1)
            loop, rest = halves()
            nc.tensor.matmul(ps[:, 0:NT], m.zeros16[:, 0:P], m.zeros16[:, 0:NT], start=True, stop=False)
            with pe.Fori(0, FULL) as i:
                for h, n in loop:
                    hist(h, n, i * 2 + h)
            for h, n in rest:
                hist(h, n, 2 * FULL + h, last=(h, n) == rest[-1])


def bucket_ranges(nc, m):
    NJ = SCP // P
    HALF = 7 * (NQ // 7) // 7 * 4
    with ExitStack() as ctx:
        sb = lambda n, s, d: ctx.enter_context(nc.sbuf_tensor(n, s, d))
        sem = lambda n: ctx.enter_context(nc.semaphore(n))
        slots = sb("slots", [P, SCD, 2], F32)
        cid = sb("chunk_id", [P, NJ], F32)
        started = sb("tiles_started", [P, NJ, NT], F32)
        tile_c = sb("tile_of_chunk", [P, NJ], F32)
        low = sb("lanes_low", [P, NJ, P], F32)
        keys = sb("keys", [P, 3, NJ], F32)
        keysT = sb("keys_t", [3 * NJ, P], F32)
        line = sb("key_line", [1, 3, SCP], F32)
        scan = sb("key_scan", [1, 3, SCP], F32)
        back = sb("key_back", [P, 3, NJ], F32)
        thr = sb("thresholds", [P, NQ], F32)
        cmp_ = sb("below", [P, 2, NQ], F32)
        lo, pr, pi = sb("first_f", [1, NQ], F32), sb("pairs_f", [1, NQ], F32), sb("pairs_i", [1, NQ], I32)
        psT = ctx.enter_context(nc.psum_tensor("lanes_ps", [P, 4, 512], F32))
        psK = psT[:, 3, 256:256 + P]
        psC = ctx.enter_context(nc.psum_tensor("count_ps", [P, 2, 2, 512], F32))
        line_dram = nc.dram_tensor("chunk_keys", [3 * NJ, P], F32).ap()
        scan_dram = nc.dram_tensor("chunk_scans", [3, SCP], F32).ap()
        s_load, s_iota, s_v, s_dst, s_T, s_keys, s_keyT, s_line, s_scan, s_cmp, s_cnt = (
            sem("br_" + n) for n in ("load", "iota", "v", "dst", "T", "keys", "keyT", "line", "scan", "cmp", "cnt"))
        block = ctx.enter_context(nc.Block())

        @block.sync
        def _(sp):
            sp.dma_start(slots[:, :, :], m.rec.rearrange("(p c) w -> p c w", p=P)).then_inc(s_load, 16)
            sp.wait_ge(s_line, 1)
            sp.dma_start(line_dram, keysT[:, :]).then_inc(s_load, 16)
            sp.wait_ge(s_load, 32)
            sp.dma_start(line[:, :, :], line_dram.rearrange("(a j) p -> (a j p)", a=3).rearrange("(o a c) -> o a c", o=1, a=3)).then_inc(s_load, 16)
            sp.wait_ge(s_scan, 1)
            sp.dma_start(scan_dram, scan[:, :, :]).then_inc(s_load, 16)
            sp.wait_ge(s_load, 64)
            sp.dma_start(back[:, :, :], scan_dram.rearrange("a (p j) -> p a j", p=P)).then_inc(s_load, 16)
            sp.wait_ge(s_load, 80)

        @block.gpsimd
        def _(gp):
            nc.gpsimd.iota(cid[:, :], pattern=[[P, NJ]], base=0, channel_multiplier=1, allow_small_or_imprecise_dtypes=True).then_inc(s_iota, 1)
            nc.gpsimd.iota(thr[:, :].rearrange("p (b t) -> p b t", t=NT), pattern=[[DB, NB], [SPAN, NT]], base=0, channel_multiplier=0, allow_small_or_imprecise_dtypes=True).then_inc(s_iota, 1)

        @block.vector
        def _(dve):
            ch = Chain(dve, s_v)
            nc.vector.memset(m.slot_src[:, :], -1.0)
            ch(nc.vector.memset(m.slot_dst[:, :], -1.0))
            dve.wait_ge(s_load, 16)
            ch(nc.vector.tensor_copy(m.slot_src[:, 0:SC], slots[:, 0:SC, 0]))
            nc.vector.tensor_copy(m.slot_dst[:, 0:SC], slots[:, 0:SC, 1]).then_inc(s_dst, 1)
            dve.wait_ge(s_iota, 2)
            ch(nc.vector.tensor_tensor(started[:, :, :], cid[:, :].unsqueeze(2).broadcast_to([P, NJ, NT]), m.first_chunk[:, :].unsqueeze(1).broadcast_to([P, NJ, NT]), ALU.is_ge))
            ch(nc.vector.tensor_reduce(tile_c[:, :], started[:, :, :], AX.X, ALU.add))
            ch(nc.vector.tensor_scalar(keys[:, 2, :], tile_c[:, :], -1.0, None, ALU.add))
            dve.wait_ge(s_T, 1)
            psd = psT[:, :, :].rearrange("p a b -> p (a b)")[:, 0:SCP].rearrange("p (j l) -> p j l", l=P)
            ch(nc.vector.tensor_reduce(keys[:, 0, :], psd, AX.X, ALU.max))
            ch(nc.vector.tensor_scalar(low[:, :, :], psd, 0.0, float(SPAN), ALU.is_lt, ALU.mult))
            ch(nc.vector.tensor_tensor(low[:, :, :], low[:, :, :], psd, ALU.add))
            ch(nc.vector.tensor_reduce(keys[:, 1, :], low[:, :, :], AX.X, ALU.min))
            for a in (0, 1):
                ch(nc.vector.scalar_tensor_tensor(keys[:, a, :], keys[:, 2, :], float(SPAN), keys[:, a, :], ALU.mult, ALU.add))
            nc.vector.tensor_copy(tile_c[:, :], keys[:, 2, :]).then_inc(s_keys, 1)
            dve.wait_ge(s_keyT, 1)
            nc.vector.tensor_copy(keysT[:, :], psK[0:3 * NJ, :]).then_inc(s_line, 1)
            dve.wait_ge(s_load, 48)
            nc.vector.tensor_tensor_scan(scan[:, 0, :], line[:, 0, :], line[:, 0, :], -1.0, ALU.max, ALU.max)
            nc.vector.tensor_tensor_scan(scan[:, 1, ::-1], line[:, 1, ::-1], line[:, 1, ::-1], float(64 * SPAN), ALU.min, ALU.min)
            nc.vector.tensor_copy(scan[:, 2, :], line[:, 2, :]).then_inc(s_scan, 1)
            ch(nc.vector.tensor_copy(m.chunk_tile[:, :], line[:, 2, 0:SC]))
            dve.wait_ge(s_load, 80)
            for a, add in ((0, 0.0), (1, float(DB))):
                ch(nc.vector.memset(cmp_[:, a, :], 0.0))
                ch(nc.vector.tensor_scalar(thr[:, :], thr[:, :], add, None, ALU.add))
                for j in range(NJ):
                    ch(nc.vector.scalar_tensor_tensor(cmp_[:, a, :], thr[:, :], back[:, a, j:j + 1], cmp_[:, a, :], ALU.is_gt, ALU.add))
            nc.vector.tensor_copy(cmp_[:, 0, 0:1], cmp_[:, 0, 0:1]).then_inc(s_cmp, 1)
            dve.wait_ge(s_cnt, 1)
            for q0, q1, k in ((0, 512, 0), (512, NQ, 1)):
                nc.vector.tensor_copy(lo[:, q0:q1], psC[0:1, 0, k, 0:q1 - q0])
                ch(nc.vector.tensor_copy(pr[:, q0:q1], psC[0:1, 1, k, 0:q1 - q0]))
            ch(nc.vector.tensor_tensor(pr[:, :], pr[:, :], lo[:, :], ALU.subtract))
            ch(nc.vector.tensor_scalar(pr[:, :], pr[:, :], 1.0, 2.0, ALU.add, ALU.max))
            ch(nc.vector.tensor_copy(pi[:, :], pr[:, :]))
            nc.vector.tensor_copy(m.ranges[0:1, :, 0], lo[:, :])
            ch(nc.vector.tensor_scalar(pi[:, :], pi[:, :], 1, None, ALU.arith_shift_right))
            nc.vector.tensor_copy(m.ranges[0:1, :, 1], pi[:, :])
            ch(nc.vector.tensor_copy(pr[:, :], pi[:, :]))
            ch(nc.vector.tensor_tensor_scan(lo[:, :], pr[:, :], pr[:, :], 0.0, ALU.add, ALU.bypass))
            nc.vector.tensor_copy(m.ranges[0:1, :, 3], lo[:, :])
            ch(nc.vector.tensor_tensor(m.ranges[0:1, :, 2], lo[:, :], pr[:, :], ALU.subtract))

        @block.tensor
        def _(pe):
            pe.wait_ge(s_dst, 1)
            psd = psT[:, :, :].rearrange("p a b -> p (a b)")
            for j in range(NJ):
                ins = nc.tensor.transpose(psd[:, j * P:(j + 1) * P], m.slot_dst[:, j * P:(j + 1) * P], m.ident[:, :])
            ins.then_inc(s_T, 1)
            pe.wait_ge(s_keys, 1)
            nc.tensor.transpose(psK[0:3 * NJ, :], keys[:, :, :].rearrange("p a j -> p (a j)"), m.ident[:, :]).then_inc(s_keyT, 1)
            pe.wait_ge(s_cmp, 1)
            for a in (0, 1):
                for q0, q1, k in ((0, 512, 0), (512, NQ, 1)):
                    ins = nc.tensor.matmul(psC[:, a, k, 0:q1 - q0], m.ones[:, :], cmp_[:, a, q0:q1], start=True, stop=True)
            ins.then_inc(s_cnt, 1)


class Mem:
    pass


def shared(nc, ctx):
    m = Mem()
    sb = lambda n, s, d: ctx.enter_context(nc.sbuf_tensor(n, s, d))
    m.iota512 = sb("iota512", [P, DB], F16)
    m.iota128h = m.iota512[:, 0:P]
    m.iota128 = sb("iota128", [P, P], F32)
    m.ones = sb("ones", [P, P], F32)
    m.before = sb("before", [P, P], F32)
    m.ident = sb("ident", [P, P], F32)
    m.zeros16 = sb("zeros16", [P, DB], F16)
    m.deg = sb("deg", [P, NT], F32)
    m.slot_src = sb("slot_src", [P, SCP], F32)
    m.slot_dst = sb("slot_dst", [P, SCP], F32)
    m.chunk_tile = sb("chunk_tile", [1, SC], I32)
    m.out_deg = sb("out_deg", [P, NQ], F32)
    m.adj = nc.dram_tensor("adjacency", [NQ // 7, P, 7 * DB], F16).ap()
    m.rec = nc.dram_tensor("records", [P * SCD, 2], F32).ap()
    return m


def for_edges(nc, m, ctx):
    sb = lambda n, s, d: ctx.enter_context(nc.sbuf_tensor(n, s, d))
    m.neg_tile = sb("neg_tile", [P, NQ], F32)
    m.neg_block = sb("neg_block", [P, NQ], F32)
    m.first_chunk = sb("first_chunk", [P, NT], F32)
    m.ranges = sb("ranges", [1, NQ, 4], I32)


def sort_edges(nc, m, src, dst):
    with ExitStack() as ctx:
        sb = lambda n, s, d: ctx.enter_context(nc.sbuf_tensor(n, s, d))
        m.empty = sb("empty", [P, 2 * SCD], F32)
        m.pair = sb("pair", [P, EC, 2], F32)
        m.dst_tile = sb("dst_tile", [P, EC], F32)
        m.dst_lo = sb("dst_low", [P, EC], F32)
        m.pos = sb("slot", [P, EC], F32)
        m.row = sb("record_row", [P, EC], I32)
        rank_edges(nc, m, src, dst)
        scatter_edges(nc, m)
    bucket_ranges(nc, m)


TG = 7
NG = NT // TG
GW = TG * P
BANKS = 4


def build_adjacency(nc, m):
    with ExitStack() as ctx:
        sb = lambda n, s, d: ctx.enter_context(nc.sbuf_tensor(n, s, d))
        sem = lambda n: ctx.enter_context(nc.semaphore(n))
        is_src = sb("is_src", [P, 2, P], F16)
        is_dst = sb("is_dst", [P, 2, DB], F16)
        stage = sb("adj_stage", [P, TG, DB], F16)
        ps = ctx.enter_context(nc.psum_tensor("adj_ps", [P, BANKS, 512], F32))
        s_hot, s_used, s_full, s_taken = (sem("ab_" + n) for n in ("hot", "used", "full", "taken"))
        s_left = [sem("ab_left0"), sem("ab_left1")]
        HALVES = ((0, 4), (4, TG))
        block = ctx.enter_context(nc.Block())

        @block.vector
        def _(dve):
            with dve.Fori(0, NQ) as q:
                first = dve.value_load(m.ranges[0:1, bass.ds(q, 1), 0], min_val=0, max_val=SC)
                pairs = dve.value_load(m.ranges[0:1, bass.ds(q, 1), 1], min_val=1, max_val=SC // 2 + 1)
                before = dve.value_load(m.ranges[0:1, bass.ds(q, 1), 2], min_val=0, max_val=NQ * SC)
                with dve.Fori(0, pairs) as i:
                    chunk = nc.s_assert_within(first + i * 2, 0, SCP - 2, skip_runtime_bounds_check_because="the ranges end at most at SC + 1")
                    for k in (0, 1):
                        c = chunk + k
                        dve.wait_ge(s_used, before * 2 + i * 2 + (k + 1))
                        nc.vector.tensor_scalar(is_src[:, k, :], m.iota128h, m.slot_src[:, bass.ds(c, 1)], col(m.neg_tile, q), ALU.subtract, ALU.is_equal)
                        nc.vector.tensor_scalar(is_dst[:, k, :], m.iota512[:, :], m.slot_dst[:, bass.ds(c, 1)], col(m.neg_block, q), ALU.subtract, ALU.is_equal).then_inc(s_hot, 1)

        @block.tensor
        def _(pe):
            pe.sem_inc(s_used, 2)
            with pe.Fori(0, NQ // TG) as g:
                for k in range(TG):
                    q = g * TG + k
                    pairs = pe.value_load(m.ranges[0:1, bass.ds(q, 1), 1], min_val=1, max_val=SC // 2 + 1)
                    before = pe.value_load(m.ranges[0:1, bass.ds(q, 1), 2], min_val=0, max_val=NQ * SC)
                    out = ps[:, k % BANKS, :]
                    pe.wait_ge(s_taken, q + 1)
                    nc.tensor.matmul(out, m.zeros16[:, 0:P], m.zeros16[:, :], start=True, stop=False)
                    with pe.Fori(0, pairs) as i:
                        for j in (0, 1):
                            pe.wait_ge(s_hot, before * 2 + i * 2 + (j + 1))
                            nc.tensor.matmul(out, is_src[:, j, :], is_dst[:, j, :], start=False, stop=False).then_inc(s_used, 1)
                    nc.tensor.matmul(ps[:, k % BANKS, 0:8], m.zeros16[:, 0:P], m.zeros16[:, 0:8], start=False, stop=True).then_inc(s_full, 1)

        @block.scalar
        def _(act):
            act.sem_inc(s_taken, BANKS - 1)
            act.sem_inc(s_left[0], 16)
            act.sem_inc(s_left[1], 16)
            with act.Fori(0, NQ // TG) as g:
                for k in range(TG):
                    q = g * TG + k
                    h = int(k >= HALVES[0][1])
                    if k == HALVES[h][0]:
                        act.wait_ge(s_left[h], g * 16 + 16)
                    act.wait_ge(s_full, q + 1)
                    ins = nc.scalar.activation(stage[:, k, :], ps[:, k % BANKS, :], ACT.Copy, accum_out=col(m.out_deg, q))
                    ins.then_inc(s_taken, 1)

        @block.sync
        def _(sp):
            with sp.Fori(0, NQ // TG) as g:
                for h, (k0, k1) in enumerate(HALVES):
                    sp.wait_ge(s_taken, g * TG + (k1 + BANKS - 1))
                    sp.dma_start(m.adj[bass.ds(g, 1), :, k0 * DB:k1 * DB].rearrange("g p w -> (g p) w"),
                                 stage[:, k0:k1, :].rearrange("p t w -> p (t w)")).then_inc(s_left[h], 16)
            for h in (0, 1):
                sp.wait_ge(s_left[h], 16 * (NQ // TG) + 16)


def aggregate(nc, m, parts, dt, name):
    with ExitStack() as ctx:
        sb = lambda n, s, d: ctx.enter_context(nc.sbuf_tensor(name + n, s, d))
        sem = lambda n: ctx.enter_context(nc.semaphore(name + n))
        ring = sb("adj_ring", [P, NG, TG * DB], F16)
        ps = ctx.enter_context(nc.psum_tensor(name + "agg_ps", [P, 512], F32))
        s_here = [sem(f"here{g}") for g in range(NG)]
        s_used, s_sum, s_out = sem("used"), sem("sum"), sem("out")
        block = ctx.enter_context(nc.Block())

        @block.sync
        def _(sp):
            def fetch(b, g):
                sp.dma_start(ring[:, g, :], m.adj[bass.ds(b * NG + g, 1), :, :].rearrange("g p w -> (g p) w")).then_inc(s_here[g], 16)
            for g in range(NG):
                fetch(0, g)
            with sp.Fori(1, NB) as b:
                for g in range(NG):
                    sp.wait_ge(s_used, b * NG + (g + 1 - NG))
                    fetch(b, g)

        @block.tensor
        def _(pe):
            pe.sem_inc(s_out, 1)
            with pe.Fori(0, NB) as b:
                pe.wait_ge(s_out, b + 1)
                for g in range(NG):
                    pe.wait_ge(s_here[g], b * 16 + 16)
                    for k in range(TG):
                        t = g * TG + k
                        for r in range(parts):
                            ins = nc.tensor.matmul(ps[:, :], m.parts[:, r, t, :].bitcast(dt), ring[:, g, k * DB:(k + 1) * DB],
                                                   start=t == 0 and r == 0, stop=t == NT - 1 and r == parts - 1)
                    ins.then_inc(s_used, 1)

        @block.scalar
        def _(act):
            act.sem_inc(s_sum, 1)
            with act.Fori(0, NB) as b:
                act.wait_ge(s_used, b * NG + NG)
                nc.scalar.activation(m.agg_t[:, bass.ds(b * DB, DB)], ps[:, :], ACT.Copy).then_inc(s_out, 1)


EPS = 1e-5
REST = N_NODES - (NT - 1) * P
TW = 2 * D + 4


def wide(t, g):
    return t[:, g * TG:(g + 1) * TG]


def spread(v, n=D):
    return v.unsqueeze(2).broadcast_to([P, v.shape[1], n])


def rows(v, k=TG):
    return v.unsqueeze(1).broadcast_to([P, k, v.shape[1]])


def load_nodes(nc, m, a):
    with ExitStack() as ctx:
        sem = lambda n: ctx.enter_context(nc.semaphore("ln_" + n))
        wo = ctx.enter_context(nc.sbuf_tensor("w_given", [P, 2, D], F32))
        rt = ctx.enter_context(nc.sbuf_tensor("sqrt_deg", [P, NT], F32))
        dg = ctx.enter_context(nc.sbuf_tensor("deg_1", [P, NT], F32))
        ps = ctx.enter_context(nc.psum_tensor("wt_ps", [P, 512], F32))
        s_load, s_v, s_T, s_rt, s_x = (sem(n) for n in ("load", "v", "T", "rt", "x"))
        block = ctx.enter_context(nc.Block())
        vec = lambda n: a[n].rearrange("(o n) -> o n", o=1)
        loads = [
            (m.xs[:, 0:NT - 1, :], a["x"][0:(NT - 1) * P, :].rearrange("(t p) d -> p t d", p=P)),
            (m.xs[0:REST, NT - 1, :], a["x"][(NT - 1) * P:N_NODES, :]),
            (m.w0[:, :], a["L0_gnn_weight"]),
            (wo[:, 0, :], a["L1_gnn_w_neigh"]), (wo[:, 1, :], a["L1_gnn_w_self"]),
            (m.w21[:, :], a["L2_gnn_W1"]), (m.w22[:, :], a["L2_gnn_W2"]),
            (m.w31[:, :, :], a["L3_gnn_W1"].rearrange("(a d) o -> d a o", a=2)),
            (m.w3l[:, :], a["L3_gnn_Wl"]),
            (m.b0[:, :], vec("L0_gnn_bias").broadcast_to([P, D])), (m.b1[:, :], vec("L1_gnn_b_self").broadcast_to([P, D])),
            (m.b21[:, :], a["L2_gnn_b1"].rearrange("(n o) -> n o", o=1)), (m.b22[:, :], vec("L2_gnn_b2").broadcast_to([P, D])),
            (m.b31[:, :], vec("L3_gnn_b1").broadcast_to([P, D])), (m.w32[:, :], a["L3_gnn_W2"].rearrange("n o -> o n").broadcast_to([P, D])),
            (m.b32[:, :], vec("L3_gnn_b2").broadcast_to([P, 1])), (m.b3l[:, :], vec("L3_gnn_bl").broadcast_to([P, D])),
        ]

        @block.sync
        def _(sp):
            sp.wait_ge(s_x, 1)
            for to, of in loads:
                sp.dma_start(to, of).then_inc(s_load, 16)
            sp.wait_ge(s_load, 16 * len(loads))

        @block.vector
        def _(dve):
            ch = Chain(dve, s_v)
            nc.vector.memset(m.xs[:, NT - 1, :], 0.0).then_inc(s_x, 1)
            ch(nc.vector.tensor_scalar(dg[:, :], m.deg[:, :], 1.0, None, ALU.max))
            nc.vector.reciprocal(m.inv_deg[:, :], dg[:, :])
            dve.wait_ge(s_rt, 1)
            ch(nc.vector.reciprocal(m.norm[:, :], rt[:, :]))
            dve.wait_ge(s_T, 1)
            nc.vector.tensor_copy(m.w1t[:, :, :], ps[:, 0:2 * D].rearrange("p (a d) -> p a d", a=2))
            dve.wait_ge(s_load, 16 * len(loads))
            ch(nc.vector.tensor_tensor(m.y[:, :, :], m.xs[:, :, :], spread(m.norm[:, :]), ALU.mult))
            for r in range(3):
                part = m.parts[:, r, :, :].bitcast(BF16)
                ch(nc.vector.tensor_copy(part, m.y[:, :, :]))
                if r < 2:
                    ch(nc.vector.tensor_tensor(m.y[:, :, :], m.y[:, :, :], part, ALU.subtract))

        @block.scalar
        def _(act):
            act.wait_ge(s_v, 1)
            nc.scalar.activation(rt[:, :], dg[:, :], ACT.Sqrt).then_inc(s_rt, 1)

        @block.tensor
        def _(pe):
            pe.wait_ge(s_load, 16 * len(loads))
            nc.tensor.transpose(ps[:, 0:D], wo[:, 0, :], m.ident[:, :])
            nc.tensor.transpose(ps[:, D:2 * D], wo[:, 1, :], m.ident[:, :]).then_inc(s_T, 1)


class Norm:

    def __init__(self, nc, m, ctx, name):
        self.nc, self.m = nc, m
        sb = lambda n, s: ctx.enter_context(nc.sbuf_tensor(name + n, s, F32))
        self.stats, self.mv = sb("bn_stats", [P, TG, 6]), sb("mean_var", [P, NT, 2])
        self.var, self.std, self.rstd = sb("var_eps", [P, NT]), sb("std", [P, NT]), sb("rstd", [P, NT])
        self.s_var, self.s_std = (ctx.enter_context(nc.semaphore(name + n)) for n in ("var", "std"))

    def statistics(self, ch, g):
        for k in range(TG):
            last = self.nc.vector.bn_stats(self.stats[:, k, :], self.m.y[:, g * TG + k, :])
        ch(last)
        for k in range(TG):
            last = self.nc.vector.bn_aggr(self.mv[:, g * TG + k, :], self.stats[:, k, :])
        ch(last)

    def apply(self, dve, ch):
        self.nc.vector.tensor_scalar(self.var[:, :], self.mv[:, :, 1], EPS, None, ALU.add).then_inc(self.s_var, 1)
        dve.wait_ge(self.s_std, 1)
        ch(self.nc.vector.reciprocal(self.rstd[:, :], self.std[:, :]))
        for t in range(NT):
            last = self.nc.vector.tensor_scalar(self.m.xs[:, t, :], self.m.y[:, t, :], self.mv[:, t, 0:1], self.rstd[:, t:t + 1], ALU.subtract, ALU.mult)
        ch(last)

    def root(self, act):
        act.wait_ge(self.s_var, 1)
        self.nc.scalar.activation(self.std[:, :], self.var[:, :], ACT.Sqrt).then_inc(self.s_std, 1)


def halves_of_group(m, v, ch, nc):
    hi, lo = (m.parts[:, r, :, :].bitcast(F16) for r in (0, 1))
    ch(nc.vector.tensor_copy(hi, m.xs[:, :, :]))
    ch(nc.vector.tensor_tensor(lo, m.xs[:, :, :], hi, ALU.subtract))


def layer0(nc, m):
    with ExitStack() as ctx:
        sem = lambda n: ctx.enter_context(nc.semaphore("l0_" + n))
        norm = Norm(nc, m, ctx, "l0_")
        t = ctx.enter_context(nc.sbuf_tensor("l0_t", [P, TG, D], F32))
        ps = ctx.enter_context(nc.psum_tensor("l0_ps", [P, 2, 2 * 512], F32))
        s_v, s_mm, s_free = sem("v"), sem("mm"), sem("free")
        block = ctx.enter_context(nc.Block())
        out = lambda g: ps[:, g % 2, 0:GW].rearrange("p (t d) -> p t d", d=D)

        @block.tensor
        def _(pe):
            for g in range(NG):
                if g >= 2:
                    pe.wait_ge(s_free, g - 1)
                for k in range(TG):
                    i = (g * TG + k) * P
                    ins = nc.tensor.matmul(out(g)[:, k, :], m.agg_t[:, i:i + P], m.w0[:, :], start=True, stop=True)
                ins.then_inc(s_mm, 1)

        @block.vector
        def _(dve):
            ch = Chain(dve, s_v)
            for g in range(NG):
                dve.wait_ge(s_mm, g + 1)
                nc.vector.tensor_tensor(t[:, :, :], out(g), spread(wide(m.norm, g)), ALU.mult).then_inc(s_free, 1)
                dve.wait_ge(s_free, g + 1)
                ch(nc.vector.tensor_tensor(t[:, :, :], t[:, :, :], rows(m.b0[:, :]), ALU.add))
                ch(nc.vector.scalar_tensor_tensor(wide(m.y, g), t[:, :, :], 0.0, wide(m.xs, g), ALU.max, ALU.add))
                norm.statistics(ch, g)
            norm.apply(dve, ch)
            halves_of_group(m, dve, ch, nc)

        @block.scalar
        def _(act):
            norm.root(act)


def layer1(nc, m):
    with ExitStack() as ctx:
        sem = lambda n: ctx.enter_context(nc.semaphore("l1_" + n))
        norm = Norm(nc, m, ctx, "l1_")
        t = ctx.enter_context(nc.sbuf_tensor("l1_t", [P, TG, D], F32))
        xt = ctx.enter_context(nc.sbuf_tensor("l1_xt", [P, 2, GW], F32))
        psx = ctx.enter_context(nc.psum_tensor("l1_psx", [P, 2 * 512], F32))
        psn = ctx.enter_context(nc.psum_tensor("l1_psn", [P, 2 * 512], F32))
        pss = ctx.enter_context(nc.psum_tensor("l1_pss", [P, 2, 2 * 512], F32))
        s_v, s_T, s_xt, s_mm, s_neigh, s_free = (sem(n) for n in ("v", "T", "xt", "mm", "neigh", "free"))
        block = ctx.enter_context(nc.Block())
        tiles = lambda p: p.rearrange("p (t d) -> p t d", d=D)

        @block.tensor
        def _(pe):
            for g in range(NG):
                if g >= 1:
                    pe.wait_ge(s_xt, g)
                for k in range(TG):
                    ins = nc.tensor.transpose(psx[:, k * P:(k + 1) * P], m.xs[:, g * TG + k, :], m.ident[:, :])
                ins.then_inc(s_T, 1)
                if g >= 1:
                    pe.wait_ge(s_neigh, g)
                if g >= 2:
                    pe.wait_ge(s_free, g - 1)
                for k in range(TG):
                    i = (g * TG + k) * P
                    nc.tensor.matmul(psn[:, k * P:(k + 1) * P], m.agg_t[:, i:i + P], m.w1t[:, 0, :], start=True, stop=True)
                pe.wait_ge(s_xt, g + 1)
                for k in range(TG):
                    ins = nc.tensor.matmul(pss[:, g % 2, k * P:(k + 1) * P], xt[:, g % 2, k * P:(k + 1) * P], m.w1t[:, 1, :], start=True, stop=True)
                ins.then_inc(s_mm, 1)

        @block.scalar
        def _(act):
            for g in range(NG):
                act.wait_ge(s_T, g + 1)
                if g >= 2:
                    act.wait_ge(s_mm, g - 1)
                nc.scalar.activation(xt[:, g % 2, :], psx[:, 0:GW], ACT.Copy).then_inc(s_xt, 1)
            norm.root(act)

        @block.vector
        def _(dve):
            ch = Chain(dve, s_v)
            for g in range(NG):
                dve.wait_ge(s_mm, g + 1)
                nc.vector.tensor_tensor(t[:, :, :], tiles(psn[:, 0:GW]), spread(wide(m.inv_deg, g)), ALU.mult).then_inc(s_neigh, 1)
                dve.wait_ge(s_neigh, g + 1)
                nc.vector.tensor_tensor(t[:, :, :], t[:, :, :], tiles(pss[:, g % 2, 0:GW]), ALU.add).then_inc(s_free, 1)
                dve.wait_ge(s_free, g + 1)
                ch(nc.vector.tensor_tensor(t[:, :, :], t[:, :, :], rows(m.b1[:, :]), ALU.add))
                ch(nc.vector.tensor_tensor(wide(m.y, g), t[:, :, :], wide(m.xs, g), ALU.add))
                norm.statistics(ch, g)
            norm.apply(dve, ch)
            halves_of_group(m, dve, ch, nc)


def layer2(nc, m):
    with ExitStack() as ctx:
        sem = lambda n: ctx.enter_context(nc.semaphore("l2_" + n))
        norm = Norm(nc, m, ctx, "l2_")
        t = ctx.enter_context(nc.sbuf_tensor("l2_t", [P, TG, D], F32))
        ht = ctx.enter_context(nc.sbuf_tensor("l2_ht", [P, GW], F32))
        gt = ctx.enter_context(nc.sbuf_tensor("l2_gt", [P, GW], F32))
        psx = ctx.enter_context(nc.psum_tensor("l2_psx", [P, 2 * 512], F32))
        psg = ctx.enter_context(nc.psum_tensor("l2_psg", [P, 2 * 512], F32))
        pso = ctx.enter_context(nc.psum_tensor("l2_pso", [P, 2 * 512], F32))
        s_v, s_T, s_h, s_g, s_gt, s_mm, s_free = (sem(n) for n in ("v", "T", "h", "g", "gt", "mm", "free"))
        block = ctx.enter_context(nc.Block())

        @block.tensor
        def _(pe):
            for g in range(NG):
                if g >= 1:
                    pe.wait_ge(s_h, g)
                for k in range(TG):
                    ins = nc.tensor.transpose(psx[:, k * P:(k + 1) * P], m.xs[:, g * TG + k, :], m.ident[:, :])
                ins.then_inc(s_T, 1)
                pe.wait_ge(s_h, g + 1)
                if g >= 1:
                    pe.wait_ge(s_gt, g)
                for c0, c1 in ((0, 512), (512, GW)):
                    ins = nc.tensor.matmul(psg[:, c0:c1], m.w21[:, :], ht[:, c0:c1], start=True, stop=True)
                ins.then_inc(s_g, 1)
                pe.wait_ge(s_gt, g + 1)
                if g >= 1:
                    pe.wait_ge(s_free, g)
                for k in range(TG):
                    ins = nc.tensor.matmul(pso[:, k * P:(k + 1) * P], gt[:, k * P:(k + 1) * P], m.w22[:, :], start=True, stop=True)
                ins.then_inc(s_mm, 1)

        @block.scalar
        def _(act):
            for g in range(NG):
                act.wait_ge(s_g, g + 1)
                if g >= 1:
                    act.wait_ge(s_mm, g)
                nc.scalar.activation(gt[:, :], psg[:, 0:GW], ACT.Relu, bias=m.b21[:, 0:1]).then_inc(s_gt, 1)
            norm.root(act)

        @block.vector
        def _(dve):
            ch = Chain(dve, s_v)

            def sums(g):
                dve.wait_ge(s_T, g + 1)
                if g >= 1:
                    dve.wait_ge(s_g, g)
                nc.vector.tensor_tensor(ht[:, :], psx[:, 0:GW], m.agg_t[:, g * GW:(g + 1) * GW], ALU.add).then_inc(s_h, 1)

            for g in range(NG):
                sums(g)
                dve.wait_ge(s_mm, g + 1)
                nc.vector.tensor_tensor(t[:, :, :], pso[:, 0:GW].rearrange("p (t d) -> p t d", d=D), rows(m.b22[:, :]), ALU.add).then_inc(s_free, 1)
                dve.wait_ge(s_free, g + 1)
                ch(nc.vector.tensor_tensor(wide(m.y, g), t[:, :, :], wide(m.xs, g), ALU.add))
                norm.statistics(ch, g)
            norm.apply(dve, ch)


def prepare_edges(nc, m):
    with ExitStack() as ctx:
        sem = lambda n: ctx.enter_context(nc.semaphore("pe_" + n))
        tab = ctx.enter_context(nc.sbuf_tensor("table_stage", [P, 2, TG, TW], F32))
        xt = ctx.enter_context(nc.sbuf_tensor("pe_xt", [P, GW], F32))
        psx = ctx.enter_context(nc.psum_tensor("pe_psx", [P, 2 * 512], F32))
        psu = ctx.enter_context(nc.psum_tensor("pe_psu", [P, 8, 2 * D], F32))
        s_v, s_T, s_xt, s_mm, s_free = (sem(n) for n in ("v", "T", "xt", "mm", "free"))
        s_put = [sem("put0"), sem("put1")]
        block = ctx.enter_context(nc.Block())

        @block.tensor
        def _(pe):
            for g in range(NG):
                if g >= 1:
                    pe.wait_ge(s_xt, g)
                for k in range(TG):
                    ins = nc.tensor.transpose(psx[:, k * P:(k + 1) * P], m.xs[:, g * TG + k, :], m.ident[:, :])
                ins.then_inc(s_T, 1)
                pe.wait_ge(s_xt, g + 1)
                if g >= 1:
                    pe.wait_ge(s_free, g)
                for k in range(TG):
                    ins = nc.tensor.matmul(psu[:, k, :], xt[:, k * P:(k + 1) * P], m.w31[:, :, :].rearrange("p a o -> p (a o)"), start=True, stop=True)
                ins.then_inc(s_mm, 1)

        @block.scalar
        def _(act):
            for g in range(NG):
                act.wait_ge(s_T, g + 1)
                if g >= 1:
                    act.wait_ge(s_mm, g)
                nc.scalar.activation(xt[:, :], psx[:, 0:GW], ACT.Copy).then_inc(s_xt, 1)

        @block.vector
        def _(dve):
            ch = Chain(dve, s_v)
            ch(nc.vector.memset(tab[:, :, :, D:D + 4], 1.0))
            for g in range(NG):
                if g >= 2:
                    dve.wait_ge(s_put[g % 2], 16 * (g // 2))
                nc.vector.tensor_copy(tab[:, g % 2, :, 0:D], wide(m.xs, g))
                dve.wait_ge(s_mm, g + 1)
                nc.vector.tensor_tensor(wide(m.u, g), psu[:, 0:TG, 0:D], rows(m.b31[:, :]), ALU.add)
                nc.vector.tensor_copy(tab[:, g % 2, :, D + 4:TW], psu[:, 0:TG, D:2 * D]).then_inc(s_free, 1)

        @block.sync
        def _(sp):
            for g in range(NG):
                sp.wait_ge(s_free, g + 1)
                sp.dma_start(m.table[g * GW:(g + 1) * GW, :].rearrange("(t p) w -> p t w", p=P), tab[:, g % 2, :, :]).then_inc(s_put[g % 2], 16)
            sp.wait_ge(s_put[0], 16 * ((NG + 1) // 2))
            sp.wait_ge(s_put[1], 16 * (NG // 2))


def edge_attention(nc, m):
    G = 4
    R = 4
    TURNS = SC // (R * G)
    GROUPS = TURNS * R
    AW = D + 1
    assert TURNS * R * G == SC
    with ExitStack() as ctx:
        sb = lambda n, s, d: ctx.enter_context(nc.sbuf_tensor("ea_" + n, s, d))
        sem = lambda n: ctx.enter_context(nc.semaphore("ea_" + n))
        at = sb("src_in_tile", [P, SC + G], F32)
        ai = sb("src_int", [P, SC], I32)
        row_of = sb("dst_row", [P, SC + 3 * G], I32)
        row_s = sb("row_stage", [P, R, G], I32)
        got = sb("gathered", [P, R, G, TW], F32)
        hot = sb("onehot", [P, R, G, P], F32)
        hot_t = sb("onehot_t", [P, 2, G, P], F32)
        hot_m = sb("onehot_mask", [P, 2, G, P], F32)
        z = sb("z", [P, 2, G, D], F32)
        dot = sb("dot", [P, 2, G], F32)
        mask = sb("mask", [P, 2, G], F32)
        pst = ctx.enter_context(nc.psum_tensor("ea_pst", [P, 2, 512], F32))
        psz = ctx.enter_context(nc.psum_tensor("ea_psz", [P, 2, 512], F32))
        psa = ctx.enter_context(nc.psum_tensor("ea_psa", [P, 2, G, 256], F32))
        s_v, s_rows, s_hot, s_T, s_hot_t, s_u, s_z, s_dot, s_relu, s_mask, s_hot_m, s_agg, s_acc, s_seen = (
            sem(n) for n in ("v", "rows", "hot", "T", "hot_t", "u", "z", "dot", "relu", "mask", "hot_m", "agg", "acc", "seen"))
        s_got = [sem(f"got{r}") for r in range(R)]
        block = ctx.enter_context(nc.Block())

        def turns(eng, step):
            for r in range(R):
                step(r, r, 0, r)
            with eng.Fori(1, TURNS) as i:
                for r in range(R):
                    step(i * R + r, r, i, R)

        def tiles(eng, n):
            return [eng.value_load(m.chunk_tile[0:1, bass.ds(n * G + k, 1)], min_val=0, max_val=NT - 1) for k in range(G)]

        @block.gpsimd
        def _(gp):
            def step(n, r, i, seen):
                gp.wait_ge(s_rows, n + 1)
                if seen >= R:
                    gp.wait_ge(s_agg, n + (1 - R))
                gp.sem_inc(s_seen, 1)
                for k in range(G):
                    nc.gpsimd.indirect_dma_start(got[:, r, k, :], None, m.table, bass.IndirectOffsetOnAxis(ap=row_s[:, r, k:k + 1], axis=0)).then_inc(s_got[r], 16)
            turns(gp, step)

        @block.vector
        def _(dve):
            ch = Chain(dve, s_v)
            nc.vector.memset(m.acc[:, :, :], 0.0)
            nc.vector.memset(at[:, :], 0.0)
            nc.vector.memset(row_of[:, :], 0)
            ch(nc.vector.tensor_copy(ai[:, :], m.slot_src[:, 0:SC]))
            ch(nc.vector.tensor_scalar(ai[:, :], ai[:, :], P - 1, None, ALU.bitwise_and))
            ch(nc.vector.tensor_copy(at[:, 0:SC], ai[:, :]))
            ch(nc.vector.tensor_scalar(m.slot_src[:, 0:SC], m.slot_src[:, 0:SC], 0.0, 1000.0, ALU.is_lt, ALU.mult))
            ch(nc.vector.tensor_tensor(at[:, 0:SC], at[:, 0:SC], m.slot_src[:, 0:SC], ALU.add))
            ch(nc.vector.tensor_scalar(m.slot_dst[:, 0:SC], m.slot_dst[:, 0:SC], 0.0, None, ALU.max))
            ch(nc.vector.tensor_copy(row_of[:, 0:SC], m.slot_dst[:, 0:SC]))

            def stage_rows(n, r):
                nc.vector.tensor_copy(row_s[:, r, :], row_of[:, bass.ds(n * G, G)]).then_inc(s_rows, 1)

            def one_hot(n, r):
                nc.vector.tensor_tensor(hot[:, r, :, :], m.iota128[:, :].unsqueeze(1).broadcast_to([P, G, P]),
                                        at[:, bass.ds(n * G, G)].unsqueeze(2).broadcast_to([P, G, P]), ALU.is_equal).then_inc(s_hot, 1)

            def masked(n, h, r, seen):
                dve.wait_ge(s_mask, n + 1)
                if seen >= 2:
                    dve.wait_ge(s_agg, n - 1)
                nc.vector.tensor_tensor(hot_m[:, h, :, :], hot[:, r, :, :], spread(mask[:, h, :], P), ALU.mult).then_inc(s_hot_m, 1)

            def accumulate(n, h):
                of = tiles(dve, n)
                dve.wait_ge(s_agg, n + 1)
                for k in range(G):
                    dst = m.acc[:, bass.ds(of[k], 1), :].rearrange("p o w -> p (o w)")
                    nc.vector.tensor_tensor(dst, dst, psa[:, h, k, 0:AW], ALU.add).then_inc(s_acc, 1)
                    dve.wait_ge(s_acc, n * G + (k + 1))

            for n in range(3):
                stage_rows(n, n)
            one_hot(0, 0)

            def step(n, r, i, seen):
                h = r % 2
                stage_rows(n + 3, (r + 3) % R)
                if seen >= 3:
                    dve.wait_ge(s_T, n - 2)
                one_hot(n + 1, (r + 1) % R)
                dve.wait_ge(s_u, n + 1)
                dve.wait_ge(s_got[r], i * (16 * G) + 16 * G)
                nc.vector.tensor_tensor(z[:, h, :, :], psz[:, h, :].rearrange("p (k d) -> p k d", d=D), got[:, r, :, D + 4:TW], ALU.add).then_inc(s_z, 1)
                dve.wait_ge(s_z, n + 1)
                nc.vector.scalar_tensor_tensor(z[:, h, :, :], z[:, h, :, :], 0.0, rows(m.w32[:, :], G), ALU.max, ALU.mult).then_inc(s_relu, 1)
                dve.wait_ge(s_relu, n + 1)
                if seen >= 2:
                    dve.wait_ge(s_mask, n - 1)
                nc.vector.tensor_reduce(dot[:, h, :], z[:, h, :, :], AX.X, ALU.add).then_inc(s_dot, 1)
                if seen >= 1:
                    masked(n - 1, 1 - h, (r + 3) % R, seen - 1)
                if seen >= 2:
                    accumulate(n - 2, h)
            turns(dve, step)
            masked(GROUPS - 1, 1, R - 1, R)
            accumulate(GROUPS - 2, 0)
            accumulate(GROUPS - 1, 1)

        @block.tensor
        def _(pe):
            def transpose(n, h, r, seen):
                pe.wait_ge(s_hot, n + 1)
                if seen >= 2:
                    pe.wait_ge(s_hot_t, n - 1)
                for k in range(G):
                    ins = nc.tensor.transpose(pst[:, h, k * P:(k + 1) * P], hot[:, r, k, :], m.ident[:, :])
                ins.then_inc(s_T, 1)

            def sums(n, h, r, seen):
                pe.wait_ge(s_hot_m, n + 1)
                if seen >= 2:
                    pe.wait_ge(s_acc, n * G - G)
                for k in range(G):
                    ins = nc.tensor.matmul(psa[:, h, k, 0:AW], hot_m[:, h, k, :], got[:, r, k, 0:AW], start=True, stop=True)
                ins.then_inc(s_agg, 1)

            def step(n, r, i, seen):
                h = r % 2
                transpose(n + 1, 1 - h, (r + 1) % R, seen + 1)
                of = tiles(pe, n)
                pe.wait_ge(s_hot_t, n + 1)
                if seen >= 2:
                    pe.wait_ge(s_z, n - 1)
                for k in range(G):
                    ins = nc.tensor.matmul(psz[:, h, k * P:(k + 1) * P], hot_t[:, h, k, :], m.u[:, bass.ds(of[k], 1), :].rearrange("p o w -> p (o w)"), start=True, stop=True)
                ins.then_inc(s_u, 1)
                if seen >= 1:
                    sums(n - 1, 1 - h, (r + 3) % R, seen - 1)
            transpose(0, 0, 0, 0)
            turns(pe, step)
            sums(GROUPS - 1, 1, R - 1, R)

        @block.scalar
        def _(act):
            def copy_t(n, h, seen):
                act.wait_ge(s_T, n + 1)
                if seen >= 2:
                    act.wait_ge(s_u, n - 1)
                nc.scalar.activation(hot_t[:, h, :, :].rearrange("p k w -> p (k w)"), pst[:, h, :], ACT.Copy).then_inc(s_hot_t, 1)

            def step(n, r, i, seen):
                h = r % 2
                copy_t(n + 1, 1 - h, seen + 1)
                act.wait_ge(s_dot, n + 1)
                if seen >= 2:
                    act.wait_ge(s_hot_m, n - 1)
                nc.scalar.activation(mask[:, h, :], dot[:, h, :], ACT.Sigmoid, bias=m.b32[:, 0:1]).then_inc(s_mask, 1)
            copy_t(0, 0, 0)
            turns(act, step)


def finish(nc, m, out):
    with ExitStack() as ctx:
        sb = lambda n, s: ctx.enter_context(nc.sbuf_tensor("fi_" + n, s, F32))
        sem = lambda n: ctx.enter_context(nc.semaphore("fi_" + n))
        norm = Norm(nc, m, ctx, "fi_")
        deg, has, fx, fa = (sb(n, [P, NT]) for n in ("deg", "has", "fx", "fa"))
        emb, t = sb("emb", [P, TG, D]), sb("t", [P, TG, D])
        et = sb("et", [P, GW])
        psx = ctx.enter_context(nc.psum_tensor("fi_psx", [P, 2 * 512], F32))
        pso = ctx.enter_context(nc.psum_tensor("fi_pso", [P, 2 * 512], F32))
        s_v, s_e, s_T, s_et, s_mm, s_free, s_out, s_st = (sem(n) for n in ("v", "e", "T", "et", "mm", "free", "out", "st"))
        block = ctx.enter_context(nc.Block())

        @block.tensor
        def _(pe):
            for g in range(NG):
                pe.wait_ge(s_e, g + 1)
                if g >= 1:
                    pe.wait_ge(s_et, g)
                for k in range(TG):
                    ins = nc.tensor.transpose(psx[:, k * P:(k + 1) * P], emb[:, k, :], m.ident[:, :])
                ins.then_inc(s_T, 1)
                pe.wait_ge(s_et, g + 1)
                if g >= 1:
                    pe.wait_ge(s_free, g)
                for k in range(TG):
                    ins = nc.tensor.matmul(pso[:, k * P:(k + 1) * P], et[:, k * P:(k + 1) * P], m.w3l[:, :], start=True, stop=True)
                ins.then_inc(s_mm, 1)

        @block.scalar
        def _(act):
            for g in range(NG):
                act.wait_ge(s_T, g + 1)
                if g >= 1:
                    act.wait_ge(s_mm, g)
                nc.scalar.activation(et[:, :], psx[:, 0:GW], ACT.Copy).then_inc(s_et, 1)
            norm.root(act)

        @block.vector
        def _(dve):
            ch = Chain(dve, s_v)
            ch(nc.vector.tensor_reduce(deg[:, :], m.out_deg[:, :].rearrange("p (b t) -> p t b", t=NT), AX.X, ALU.add))
            ch(nc.vector.tensor_scalar(has[:, :], deg[:, :], 0.0, 0.5, ALU.is_gt, ALU.mult))
            ch(nc.vector.tensor_scalar(fx[:, :], has[:, :], -1.0, 1.0, ALU.mult, ALU.add))
            ch(nc.vector.tensor_scalar(fa[:, :], m.acc[:, :, D], 1e-9, None, ALU.add))
            ch(nc.vector.reciprocal(fa[:, :], fa[:, :]))
            ch(nc.vector.tensor_tensor(fa[:, :], fa[:, :], has[:, :], ALU.mult))
            for g in range(NG):
                if g >= 1:
                    dve.wait_ge(s_T, g)
                nc.vector.tensor_tensor(emb[:, :, :], wide(m.xs, g), spread(wide(fx, g)), ALU.mult)
                ch(nc.vector.tensor_tensor(t[:, :, :], wide(m.acc, g)[:, :, 0:D], spread(wide(fa, g)), ALU.mult))
                nc.vector.tensor_tensor(emb[:, :, :], emb[:, :, :], t[:, :, :], ALU.add).then_inc(s_e, 1)
                dve.wait_ge(s_mm, g + 1)
                nc.vector.tensor_tensor(t[:, :, :], pso[:, 0:GW].rearrange("p (t d) -> p t d", d=D), rows(m.b3l[:, :]), ALU.add).then_inc(s_free, 1)
                dve.wait_ge(s_free, g + 1)
                ch(nc.vector.scalar_tensor_tensor(wide(m.y, g), t[:, :, :], 0.0, wide(m.xs, g), ALU.max, ALU.add))
                norm.statistics(ch, g)
            norm.apply(dve, ch)
            nc.vector.tensor_copy(t[:, 0, :], t[:, 0, :]).then_inc(s_st, 1)

        @block.sync
        def _(sp):
            sp.wait_ge(s_st, 1)
            sp.dma_start(out[0:(NT - 1) * P, :].rearrange("(t p) d -> p t d", p=P), m.xs[:, 0:NT - 1, :]).then_inc(s_out, 16)
            sp.dma_start(out[(NT - 1) * P:N_NODES, :], m.xs[0:REST, NT - 1, :]).then_inc(s_out, 16)
            sp.wait_ge(s_out, 32)


def program(nc, a, out):
    with ExitStack() as ctx:
        m = shared(nc, ctx)
        with ExitStack() as edges:
            for_edges(nc, m, edges)
            sort_edges(nc, m, a["src"], a["dst"])
            build_adjacency(nc, m)
        sb = lambda n, s: ctx.enter_context(nc.sbuf_tensor(n, s, F32))
        m.agg_t = sb("agg_t", [P, NB * DB])
        m.parts = ctx.enter_context(nc.sbuf_tensor("parts", [P, 3, NT, P], U16))
        m.xs = sb("xs", [P, NT, D])
        m.w0, m.w21, m.w22, m.w3l = (sb(n, [P, D]) for n in ("w0", "w21", "w22", "w3l"))
        m.w1t, m.w31 = sb("w1t", [P, 2, D]), sb("w31", [P, 2, D])
        m.b0, m.b1, m.b22, m.b31, m.w32, m.b3l = (sb(n, [P, D]) for n in ("b0", "b1", "b22", "b31", "w32", "b3l"))
        m.b21, m.b32 = sb("b21", [P, 1]), sb("b32", [P, 1])
        m.inv_deg, m.norm = sb("inv_deg", [P, NT]), sb("norm", [P, NT])

        def with_y(step, *args):
            with nc.sbuf_tensor(step.__name__ + "_y", [P, NT, D], F32) as y:
                m.y = y
                step(nc, m, *args)

        with_y(load_nodes, a)
        aggregate(nc, m, 3, BF16, "a0_")
        with_y(layer0)
        aggregate(nc, m, 2, F16, "a1_")
        with_y(layer1)
        aggregate(nc, m, 2, F16, "a2_")
        with_y(layer2)
        m.u = m.parts[:, 0:2, :, :].rearrange("p r t d -> p (r t d)").bitcast(F32).rearrange("p (t d) -> p t d", d=D)
        m.acc = m.agg_t[:, 0:NT * (D + 1)].rearrange("p (t w) -> p t w", w=D + 1)
        m.table = nc.dram_tensor("edge_table", [NP, TW], F32).ap()
        prepare_edges(nc, m)
        edge_attention(nc, m)
        with_y(finish, out)


def kernel(x, src, dst, L0_gnn_weight, L0_gnn_bias, L1_gnn_w_neigh, L1_gnn_w_self, L1_gnn_b_self, L2_gnn_W1, L2_gnn_b1,
           L2_gnn_W2, L2_gnn_b2, L3_gnn_W1, L3_gnn_b1, L3_gnn_W2, L3_gnn_b2, L3_gnn_Wl, L3_gnn_bl):
    import concourse.bacc as bacc
    import numpy as np
    from concourse.bass_utils import run_bass_kernel_spmd

    given = dict(locals())
    names = ["x", "src", "dst", "L0_gnn_weight", "L0_gnn_bias", "L1_gnn_w_neigh", "L1_gnn_w_self", "L1_gnn_b_self",
             "L2_gnn_W1", "L2_gnn_b1", "L2_gnn_W2", "L2_gnn_b2", "L3_gnn_W1", "L3_gnn_b1", "L3_gnn_W2", "L3_gnn_b2",
             "L3_gnn_Wl", "L3_gnn_bl"]
    nc = bacc.Bacc("TRN2", target_bir_lowering=False, num_devices=1)
    arrays = {n: np.ascontiguousarray(given[n]) for n in names}
    a = {n: nc.dram_tensor(n, v.shape, mybir.dt.from_np(v.dtype), kind="ExternalInput").ap() for n, v in arrays.items()}
    out = nc.dram_tensor("out", (N_NODES, D), F32, kind="ExternalOutput").ap()
    program(nc, a, out)
    r = run_bass_kernel_spmd(nc, [arrays], core_ids=[0])
    return r.results[0]["out"]
```
